# Optimizing a Trainium2 kernel written in Bass

```python
import numpy as np
import jax
import jax.numpy as jnp

def _softmax(x, axis=-1):
    return jax.nn.softmax(x, axis=axis)

def _gelu(x):
    return jax.nn.gelu(x, approximate=True)

def _silu(x):
    return jax.nn.silu(x)

def _sigmoid(x):
    return jax.nn.sigmoid(x)

def _layernorm(x, axis=-1, eps=1e-05):
    m = jnp.mean(x, axis=axis, keepdims=True)
    v = jnp.var(x, axis=axis, keepdims=True)
    return (x - m) / jnp.sqrt(v + eps)

def _scatter_add(tgt, idx, src, axis=0):
    return tgt.at[idx].add(src)

def _segment_sum(src, seg, n):
    return jax.ops.segment_sum(src, seg, n)
kernel_name = 'mk_flamingo_gated_d1_seqx_r4_5e4576'

def setup_inputs(seed: int=0):
    np.random.seed(seed)
    _w = jnp.asarray

    def _rec_inputs():
        import jax
        import jax.numpy as jnp
        _rk = jax.random.key(seed)
        x = -0.0001661 + 0.9999 * jax.random.normal(jax.random.fold_in(_rk, 1), (8, 512, 512), jnp.float32)
        _lenS = 512 - jax.random.randint(jax.random.fold_in(_rk, 7), (8,), 0, max(1, 512 // 4) + 1, jnp.int32)
        _lenS2 = 1601 - jax.random.randint(jax.random.fold_in(_rk, 8), (8,), 0, max(1, 1601 // 4) + 1, jnp.int32)
        _ctx_2048P = jax.random.normal(jax.random.fold_in(_rk, 11), (8, 16, 512), jnp.float32)
        _ctx_2048c = jax.random.dirichlet(jax.random.fold_in(_rk, 511), 0.3 * jnp.ones((16,), jnp.float32), (8, 1601))
        _ctx_2048t = jnp.einsum('bsk,bkd->bsd', _ctx_2048c, _ctx_2048P)
        _ctx_2048t = _ctx_2048t * jax.lax.rsqrt(jnp.mean(jnp.square(_ctx_2048t)) + 1e-12) * 0.953939
        ctx_2048 = -0.00016346 + 1.00032 * (_ctx_2048t + 0.3 * jax.random.normal(jax.random.fold_in(_rk, 611), (8, 1601, 512), jnp.float32))
        _g = jax.random.normal(jax.random.fold_in(_rk, 9001), (2, 1), jnp.float32)
        _g = jnp.sign(_g) * jnp.maximum(jnp.abs(_g), 1.0) + (_g == 0) * 1.0
        g_xattn = _g[0]
        g_ffn = _g[1]
        return (x, ctx_2048, _lenS2, g_xattn, g_ffn)
    x, ctx_2048, _lenS2, g_xattn, g_ffn = _rec_inputs()

    def _L0_xattn_setup():
        import jax, jax.numpy as jnp
        import numpy as np
        DIM = 512
        HEADS = 16
        HEAD_DIM = DIM // HEADS
        EPS = 1e-06
        IMG_TOKENS = 257
        B, L1, L2 = (2, 1024, 769)
        SCALE = 1.0 / np.sqrt(HEAD_DIM).astype(np.float32)

        def rms_norm(x, g):
            return x * jax.lax.rsqrt(jnp.mean(x * x, axis=-1, keepdims=True) + EPS) * g

        def attention(q, k, v, kv_mask=None):
            s = jnp.einsum('bqhd,bkhd->bhqk', q, k) * SCALE
            if kv_mask is not None:
                s = jnp.where(kv_mask[:, None, None, :], s, jnp.float32(-1000000000.0))
            p = jax.nn.softmax(s, axis=-1)
            return jnp.einsum('bhqk,bkhd->bqhd', p, v)
        key = jax.random.key(seed)
        ks = jax.random.split(key, 20)
        std = 0.02

        def lin(i):
            return (jax.random.normal(ks[i], (DIM, DIM), jnp.float32) * std, jnp.zeros((DIM,), jnp.float32))
        w_q, b_q = lin(0)
        w_k, b_k = lin(1)
        w_v, b_v = lin(2)
        w_k_img, b_k_img = lin(3)
        w_v_img, b_v_img = lin(4)
        w_o, b_o = lin(5)
        return {'x': jax.random.normal(ks[6], (B, L1, DIM), jnp.float32), 'context': jax.random.normal(ks[7], (B, L2, DIM), jnp.float32), 'context_lens': jax.random.randint(ks[8], (B,), 64, 513, jnp.int64 if jax.config.jax_enable_x64 else jnp.int32), 'w_q': w_q, 'b_q': b_q, 'w_k': w_k, 'b_k': b_k, 'w_v': w_v, 'b_v': b_v, 'w_k_img': w_k_img, 'b_k_img': b_k_img, 'w_v_img': w_v_img, 'b_v_img': b_v_img, 'w_o': w_o, 'b_o': b_o, 'g_q': jnp.ones((DIM,), jnp.float32), 'g_k': jnp.ones((DIM,), jnp.float32), 'g_k_img': jnp.ones((DIM,), jnp.float32)}
    _L0_xattn_all = _L0_xattn_setup()
    _L0_xattn_in = {k: v for k, v in _L0_xattn_all.items() if k in ('w_q', 'b_q', 'w_k', 'b_k', 'w_v', 'b_v', 'w_k_img', 'b_k_img', 'w_v_img', 'b_v_img', 'w_o', 'b_o', 'g_q', 'g_k', 'g_k_img')}
    del _L0_xattn_all

    def _L0_ffn_setup():
        import jax, jax.numpy as jnp
        import numpy as np
        THRESHOLD = 0.05
        ACT_BITS = 4
        QMAX = 2 ** (ACT_BITS - 1) - 1
        EPS = 1e-08

        def ternarize(W, threshold):
            absW = jnp.abs(W)
            delta = threshold * jnp.max(absW)
            mask = absW > delta
            n = jnp.maximum(jnp.sum(mask), 1)
            alpha = jnp.sum(jnp.where(mask, absW, 0.0)) / n
            Wt = alpha * jnp.sign(W) * mask
            return W + jax.lax.stop_gradient(Wt - W)

        def ternary_linear(x, W, b, threshold=THRESHOLD):
            Wq = ternarize(W, threshold)
            return jnp.einsum('bsd,hd->bsh', x, Wq) + b

        def fp4_activation(x):
            scale = jnp.max(jnp.abs(x)) / QMAX + EPS
            q = jnp.clip(jnp.round(x / scale), -QMAX, QMAX) * scale
            return x + jax.lax.stop_gradient(q - x)
        key = jax.random.key(seed)
        k1, k2, k3, k4, k5 = jax.random.split(key, 5)
        B, S, D, H = (2, 1024, 512, 2048)
        x = jax.random.normal(k1, (B, S, D), dtype=jnp.float32)
        W1 = jax.random.normal(k2, (H, D), dtype=jnp.float32) * (1.0 / np.sqrt(D))
        b1 = jax.random.normal(k3, (H,), dtype=jnp.float32) * 0.02
        W2 = jax.random.normal(k4, (D, H), dtype=jnp.float32) * (1.0 / np.sqrt(H))
        b2 = jax.random.normal(k5, (D,), dtype=jnp.float32) * 0.02
        return {'x': x, 'W1': W1, 'b1': b1, 'W2': W2, 'b2': b2}
    _L0_ffn_all = _L0_ffn_setup()
    _L0_ffn_in = {k: v for k, v in _L0_ffn_all.items() if k in ('W1', 'b1', 'W2', 'b2')}
    del _L0_ffn_all
    return {'x': x, 'ctx_2048': ctx_2048, '_lenS2': _lenS2, 'g_xattn': g_xattn, 'g_ffn': g_ffn, 'L0_xattn_w_q': _L0_xattn_in['w_q'], 'L0_xattn_b_q': _L0_xattn_in['b_q'], 'L0_xattn_w_k': _L0_xattn_in['w_k'], 'L0_xattn_b_k': _L0_xattn_in['b_k'], 'L0_xattn_w_v': _L0_xattn_in['w_v'], 'L0_xattn_b_v': _L0_xattn_in['b_v'], 'L0_xattn_w_k_img': _L0_xattn_in['w_k_img'], 'L0_xattn_b_k_img': _L0_xattn_in['b_k_img'], 'L0_xattn_w_v_img': _L0_xattn_in['w_v_img'], 'L0_xattn_b_v_img': _L0_xattn_in['b_v_img'], 'L0_xattn_w_o': _L0_xattn_in['w_o'], 'L0_xattn_b_o': _L0_xattn_in['b_o'], 'L0_xattn_g_q': _L0_xattn_in['g_q'], 'L0_xattn_g_k': _L0_xattn_in['g_k'], 'L0_xattn_g_k_img': _L0_xattn_in['g_k_img'], 'L0_ffn_W1': _L0_ffn_in['W1'], 'L0_ffn_b1': _L0_ffn_in['b1'], 'L0_ffn_W2': _L0_ffn_in['W2'], 'L0_ffn_b2': _L0_ffn_in['b2']}

def reference(x, ctx_2048, _lenS2, g_xattn, g_ffn, L0_xattn_w_q, L0_xattn_b_q, L0_xattn_w_k, L0_xattn_b_k, L0_xattn_w_v, L0_xattn_b_v, L0_xattn_w_k_img, L0_xattn_b_k_img, L0_xattn_w_v_img, L0_xattn_b_v_img, L0_xattn_w_o, L0_xattn_b_o, L0_xattn_g_q, L0_xattn_g_k, L0_xattn_g_k_img, L0_ffn_W1, L0_ffn_b1, L0_ffn_W2, L0_ffn_b2):
    import jax
    import jax.numpy as jnp

    def _L0_xattn_ref(x, context, context_lens, w_q, b_q, w_k, b_k, w_v, b_v, w_k_img, b_k_img, w_v_img, b_v_img, w_o, b_o, g_q, g_k, g_k_img):
        import jax, jax.numpy as jnp
        import numpy as np
        DIM = 512
        HEADS = 16
        HEAD_DIM = DIM // HEADS
        EPS = 1e-06
        IMG_TOKENS = 257
        B, L1, L2 = (2, 1024, 769)
        SCALE = 1.0 / np.sqrt(HEAD_DIM).astype(np.float32)

        def rms_norm(x, g):
            return x * jax.lax.rsqrt(jnp.mean(x * x, axis=-1, keepdims=True) + EPS) * g

        def attention(q, k, v, kv_mask=None):
            s = jnp.einsum('bqhd,bkhd->bhqk', q, k) * SCALE
            if kv_mask is not None:
                s = jnp.where(kv_mask[:, None, None, :], s, jnp.float32(-1000000000.0))
            p = jax.nn.softmax(s, axis=-1)
            return jnp.einsum('bhqk,bkhd->bqhd', p, v)
        b = x.shape[0]
        ctx_img = context[:, :IMG_TOKENS]
        ctx_txt = context[:, IMG_TOKENS:]
        q = rms_norm(x @ w_q.T + b_q, g_q).reshape(b, -1, HEADS, HEAD_DIM)
        k = rms_norm(ctx_txt @ w_k.T + b_k, g_k).reshape(b, -1, HEADS, HEAD_DIM)
        v = (ctx_txt @ w_v.T + b_v).reshape(b, -1, HEADS, HEAD_DIM)
        k_img = rms_norm(ctx_img @ w_k_img.T + b_k_img, g_k_img).reshape(b, -1, HEADS, HEAD_DIM)
        v_img = (ctx_img @ w_v_img.T + b_v_img).reshape(b, -1, HEADS, HEAD_DIM)
        txt_len = ctx_txt.shape[1]
        kv_mask = jnp.arange(txt_len)[None, :] < context_lens[:, None]
        img_x = attention(q, k_img, v_img)
        txt_x = attention(q, k, v, kv_mask)
        out = (txt_x + img_x).reshape(b, -1, DIM)
        return out @ w_o.T + b_o

    def _L0_ffn_ref(x, W1, b1, W2, b2):
        import jax, jax.numpy as jnp
        import numpy as np
        THRESHOLD = 0.05
        ACT_BITS = 4
        QMAX = 2 ** (ACT_BITS - 1) - 1
        EPS = 1e-08

        def ternarize(W, threshold):
            absW = jnp.abs(W)
            delta = threshold * jnp.max(absW)
            mask = absW > delta
            n = jnp.maximum(jnp.sum(mask), 1)
            alpha = jnp.sum(jnp.where(mask, absW, 0.0)) / n
            Wt = alpha * jnp.sign(W) * mask
            return W + jax.lax.stop_gradient(Wt - W)

        def ternary_linear(x, W, b, threshold=THRESHOLD):
            Wq = ternarize(W, threshold)
            return jnp.einsum('bsd,hd->bsh', x, Wq) + b

        def fp4_activation(x):
            scale = jnp.max(jnp.abs(x)) / QMAX + EPS
            q = jnp.clip(jnp.round(x / scale), -QMAX, QMAX) * scale
            return x + jax.lax.stop_gradient(q - x)
        h = ternary_linear(x, W1, b1)
        h = jax.nn.gelu(h, approximate=False)
        y = ternary_linear(h, W2, b2)
        return fp4_activation(y)
    x = x + jnp.tanh(g_xattn[0]) * _L0_xattn_ref(_layernorm(x, axis=-1), ctx_2048, _lenS2, L0_xattn_w_q, L0_xattn_b_q, L0_xattn_w_k, L0_xattn_b_k, L0_xattn_w_v, L0_xattn_b_v, L0_xattn_w_k_img, L0_xattn_b_k_img, L0_xattn_w_v_img, L0_xattn_b_v_img, L0_xattn_w_o, L0_xattn_b_o, L0_xattn_g_q, L0_xattn_g_k, L0_xattn_g_k_img)
    x = x + jnp.tanh(g_ffn[0]) * _L0_ffn_ref(_layernorm(x, axis=-1), L0_ffn_W1, L0_ffn_b1, L0_ffn_W2, L0_ffn_b2)
    return x

_drawn_inputs = setup_inputs


def setup_inputs(seed=0):
    import zlib

    import numpy as np

    out = dict(_drawn_inputs(seed))
    spreads = {'L0_xattn_b_q': (0.0, 0.305),
     'L0_xattn_b_k': (0.0, 0.8),
     'L0_xattn_b_v': (0.0, 0.1),
     'L0_xattn_b_k_img': (0.0, 0.792),
     'L0_xattn_b_v_img': (0.0, 0.1),
     'L0_xattn_b_o': (0.0, 0.1),
     'L0_xattn_g_q': (1.0, 0.6),
     'L0_xattn_g_k': (1.0, 0.6),
     'L0_xattn_g_k_img': (1.0, 0.6)}
    factors = {}
    for name, (base, spread) in spreads.items():
        noise = np.random.default_rng([zlib.crc32(name.encode()), seed]).standard_normal(out[name].shape)
        drawn = base * np.exp(spread * noise) if base else spread * noise
        out[name] = jnp.asarray(drawn.astype(out[name].dtype))
    for name, factor in factors.items():
        out[name] = (out[name] * factor).astype(out[name].dtype)
    return out
```

```python
from contextlib import ExitStack

import concourse.bass as bass
from concourse import mybir

ALU = mybir.AluOpType
ACT = mybir.ActivationFunctionType
AX = mybir.AxisListType
F32 = mybir.dt.float32
F32R = mybir.dt.float32r
BF16 = mybir.dt.bfloat16
I32 = mybir.dt.int32
RMAX = bass.bass_isa.ReduceOp.max
RADD = bass.bass_isa.ReduceOp.add

P = 128
B, SQ, D = 8, 512, 512
SK, NIMG = 1601, 257
NTXT = SK - NIMG
HD = 32
HG = P // HD
NG = D // P
GROUPS = B * NG
FF = 2048
NF = FF // P
KT = (SK + P - 1) // P
KLAST = SK - (KT - 1) * P
MIX = NIMG // P
QT = SQ // P
SCALE = HD ** -0.5
RMS_EPS, LN_EPS, ACT_EPS = 1e-6, 1e-5, 1e-8
MASKED = float(2 ** 60)
QMAX = 7.0
MAGIC = 1.5 * 2 ** 23
THRESHOLD = 0.05
AUX = 5


class Names:

    def __init__(self, nc, ctx, prefix):
        self.nc, self.ctx, self.prefix = nc, ctx, prefix

    def sb(self, name, shape, dt=F32):
        return self.ctx.enter_context(self.nc.sbuf_tensor(f"{self.prefix}_{name}", shape, dt))

    def banks(self, name, n):
        return self.ctx.enter_context(self.nc.psum_tensor(f"{self.prefix}_{name}", [P, n, 512], F32))

    def sem(self, name):
        return self.ctx.enter_context(self.nc.semaphore(f"{self.prefix}_{name}"))


def split_matmuls(nc, out, stat_hi, stat_lo, move_hi, move_lo, chunks):
    last = None
    for c in range(chunks):
        pairs = ((stat_hi, move_hi), (stat_hi, move_lo), (stat_lo, move_hi))
        for j, (s, m) in enumerate(pairs):
            last = nc.tensor.matmul(out, s(c), m(c), start=(c == 0 and j == 0),
                                    stop=(c == chunks - 1 and j == 2))
    return last


def prepare_weights(nc, ident, sources, parts, tag):
    with ExitStack() as ctx:
        a = Names(nc, ctx, tag)
        nat = [a.sb(f"nat{w}", [P, NG, D]) for w in range(len(sources))]
        ps = a.banks("ps", 8)
        loaded = [a.sem(f"loaded{w}") for w in range(len(sources))]
        ident_set, turned, high_done, low_done = (a.sem(x) for x in ("ident_set", "turned", "high_done", "low_done"))
        jobs = [(w, c) for w in range(len(sources)) for c in range(NG)]
        block = ctx.enter_context(nc.Block())

        @block.sync
        def _(sp):
            for w, src in enumerate(sources):
                sp.dma_start(nat[w][:], src.rearrange("(o p) i -> p o i", p=P)).then_inc(loaded[w], 16)

        @block.gpsimd
        def _(pool):
            pool.memset(ident[:], 0.0).then_inc(ident_set, 1)
            pool.wait_ge(ident_set, 1)
            pool.affine_select(out=ident[:], in_=ident[:], compare_op=ALU.not_equal, fill=1.0, base=0,
                               pattern=[[-1, P]], channel_multiplier=1).then_inc(ident_set, 1)

        @block.tensor
        def _(pe):
            pe.wait_ge(ident_set, 2)
            for n, (w, c) in enumerate(jobs):
                if c == 0:
                    pe.wait_ge(loaded[w], 16)
                if n >= 8:
                    pe.wait_ge(low_done, n - 7)
                for o in range(NG):
                    last = pe.transpose(ps[:, n % 8, o * P:(o + 1) * P], nat[w][:, o, c * P:(c + 1) * P], ident[:])
                last.then_inc(turned, 1)

        @block.scalar
        def _(act):
            for n, (w, c) in enumerate(jobs):
                act.wait_ge(turned, n + 1)
                act.activation(parts[w][0][:, c, :], ps[:, n % 8, :], ACT.Copy).then_inc(high_done, 1)

        @block.vector
        def _(dve):
            for n, (w, c) in enumerate(jobs):
                dve.wait_ge(high_done, n + 1)
                dve.tensor_tensor(parts[w][1][:, c, :], ps[:, n % 8, :], parts[w][0][:, c, :].bitcast(F32),
                                  ALU.subtract).then_inc(low_done, 1)


class Seg:

    def __init__(self, kind, n, T, stores):
        self.kind, self.n, self.T, self.stores = kind, n, T, stores


class Tile:
    def __init__(self, segs, s, i, k):
        self.segs, self.s, self.i, self.k = segs, s, i, k
        self.seg = seg = segs[s]
        base = sum(x.n * x.T for x in segs[:s])
        assert seg.T % 2 == 0 or seg.n == 1
        self.n = base + k + i * seg.T
        self.par = (base + k) % 2
        self.half = (base + k) // 2 + i * (seg.T // 2)
        self.next_half = (base + k + 1) // 2 + i * (seg.T // 2)
        before = 0
        for j, x in enumerate(segs[:s]):
            b0 = sum(y.n * y.T for y in segs[:j])
            before += x.stores * sum((b0 + t) % 2 == self.par for t in range(x.n * x.T))
        self.stored_before = 16 * (before + (k // 2) * seg.stores) + i * (16 * seg.stores * (seg.T // 2))
        self.stored = self.stored_before + 16 * seg.stores
        self.first = isinstance(self.n, int) and self.n == 0
        self.last = isinstance(self.n, int) and self.n == sum(x.n * x.T for x in segs) - 1

    def prev(self):
        if self.k > 0:
            return Tile(self.segs, self.s, self.i, self.k - 1)
        if isinstance(self.i, int) and self.i == 0:
            p = self.segs[self.s - 1]
            return Tile(self.segs, self.s - 1, p.n - 1, p.T - 1)
        return Tile(self.segs, self.s, self.i - 1, self.seg.T - 1)


def walk(eng, segs, step):
    for s, seg in enumerate(segs):
        for k in range(seg.T):
            step(Tile(segs, s, 0, k))
        end = seg.n - 1 if s == len(segs) - 1 else seg.n
        if end > 1:
            with eng.Fori(1, end) as i:
                for k in range(seg.T):
                    step(Tile(segs, s, i, k))
        if end < seg.n and seg.n > 1:
            for k in range(seg.T):
                step(Tile(segs, s, seg.n - 1, k))


def rstd_steps(dve, eng_col, ss, step, scale, eps, sq_done, sq_value, base, extra):
    V, R0, T1, T2, R = range(5)
    col = lambda c: eng_col[:, c:c + 1]
    dve.tensor_scalar(col(V), ss, scale, eps, ALU.mult, ALU.add).then_inc(step, 1)
    dve.wait_ge(sq_done, sq_value)
    dve.reciprocal(col(R0), col(5)).then_inc(step, 1)
    dve.wait_ge(step, base + 2)
    dve.scalar_tensor_tensor(col(T1), col(R0), col(R0), col(V), ALU.mult, ALU.mult).then_inc(step, 1)
    dve.wait_ge(step, base + 3)
    dve.tensor_scalar(col(T2), col(T1), -0.5, 1.5, ALU.mult, ALU.add).then_inc(step, 1)
    dve.wait_ge(step, base + 4)
    dve.scalar_tensor_tensor(col(R), col(T2), col(R0), extra, ALU.mult, ALU.mult).then_inc(step, 1)
    dve.wait_ge(step, base + 5)
    return col(R)


def project(nc, ident, x, ctx_in, lens, weights, rows, scratch):
    kh_d, kl_d, v_d, qh_d, ql_d, aux_d = scratch
    segs = [Seg("img", B, 2, 3), Seg("extra", 1, 1, 2 * NG + 1), Seg("txt", B, 10, 3), Seg("rem", 1, 4, 6), Seg("q", B, QT, 2)]
    TXT_FULL = 10
    REM = NTXT - TXT_FULL * P
    khv, klv = (t.rearrange("(b c) d k -> b d c k", c=NG) for t in (kh_d, kl_d))
    qhv, qlv = (t.rearrange("(b c) d q -> b d c q", c=NG) for t in (qh_d, ql_d))
    vv = v_d.rearrange("(b c) k d -> b k c d", c=NG)
    with ExitStack() as ctx:
        a = Names(nc, ctx, "pj")
        xin = [a.sb(f"xin{p}", [P, D]) for p in range(2)]
        xh = [a.sb(f"xh{p}", [P, D], F32R) for p in range(2)]
        xl = [a.sb(f"xl{p}", [P, D], F32R) for p in range(2)]
        kb = [a.sb(f"kb{p}", [P, D]) for p in range(2)]
        kn = [a.sb(f"kn{p}", [P, D]) for p in range(2)]
        kh = [a.sb(f"kh{p}", [P, D], F32R) for p in range(2)]
        kl = [a.sb(f"kl{p}", [P, D], F32R) for p in range(2)]
        vs = [a.sb(f"vs{p}", [P, D]) for p in range(2)]
        squares = a.sb("squares", [P, D])
        cols = [a.sb(f"cols{p}", [P, 8]) for p in range(2)]
        lcols = [a.sb(f"lcols{p}", [P, 16]) for p in range(2)]
        bias = {k: a.sb(f"bias_{k}", [P, D]) for k in ("img", "txt", "q")}
        gain = {k: a.sb(f"gain_{k}", [P, D]) for k in ("img", "txt", "q")}
        one = a.sb("one", [P, 1])
        len_i = a.sb("len_i", [P, B], I32)
        len_f = a.sb("len_f", [P, B])
        idx_i = a.sb("idx_i", [P, TXT_FULL + 1], I32)
        idx_f = a.sb("idx_f", [P, TXT_FULL + 1])
        valid = a.sb("valid", [P, B * TXT_FULL])
        validr = a.sb("validr", [P, B // 2])
        klen_i = a.sb("klen_i", [B, 1], I32)
        klen_f = a.sb("klen_f", [B, 1])
        kidx_i = a.sb("kidx_i", [B, SK], I32)
        kidx_f = a.sb("kidx_f", [B, SK])
        aux = a.sb("aux", [B, AUX, SK])
        psx, psk, psv, pst = (a.banks(n, 2) for n in ("psx", "psk", "psv", "pst"))
        x_ready = [a.sem(f"x_ready{p}") for p in range(2)]
        x_landed = [a.sem(f"x_landed{p}") for p in range(2)]
        stored = [a.sem(f"stored{p}") for p in range(2)]
        stats = [a.sb(f"stats{p}", [P, 6]) for p in range(2)]
        Q0 = sum(s.n * s.T for s in segs[:-1])
        names = ("rem_landed const_in tx_done xh_done xl_done mmk_done mmv_done kb_done ss_done sq_done "
                 "step kn_done tk_done kh_done kl_done v_done ln_step lnsq_done idx_set len_set valid_set aux_set aux_out").split()
        S = {n: a.sem(n) for n in names}
        block = ctx.enter_context(nc.Block())
        g = lambda kind: "txt" if kind == "rem" else "img" if kind == "extra" else kind

        @block.sync
        def _(sp):
            for t in ("img", "txt", "q"):
                sp.dma_start(bias[t][:], rows["b_" + t].partition_broadcast(P)).then_inc(S["const_in"], 16)
                sp.dma_start(gain[t][:], rows["g_" + t].partition_broadcast(P)).then_inc(S["const_in"], 16)
            sp.dma_start(len_i[:], lens.partition_broadcast(P)).then_inc(S["const_in"], 16)
            sp.dma_start(klen_i[:], lens.rearrange("(b o) -> b o", o=1), allow_slow_non_contiguous=True).then_inc(S["const_in"], 16)

            def load(t):
                if not (isinstance(t.n, int) and t.n < 2):
                    sp.wait_ge(S["tx_done"], t.n - 1)
                kind, i, k, p = t.seg.kind, t.i, t.k, t.par
                if kind == "img":
                    sp.dma_start(xin[p][:], ctx_in[i, k * P:(k + 1) * P, :]).then_inc(x_ready[p], 16)
                elif kind == "extra":
                    sp.dma_start(xin[p][0:B, :], ctx_in[:, NIMG - 1, :]).then_inc(x_ready[p], 16)
                elif kind == "txt":
                    k0 = NIMG + k * P
                    sp.dma_start(xin[p][:], ctx_in[i, k0:k0 + P, :]).then_inc(x_ready[p], 16)
                elif kind == "rem":
                    for r in range(2):
                        sp.dma_start(xin[p][r * REM:(r + 1) * REM, :], ctx_in[2 * k + r, SK - REM:SK, :]).then_inc(S["rem_landed"], 16)
                    sp.wait_ge(S["rem_landed"], 32 * (k + 1))
                    sp.sem_inc(x_ready[p], 16)
                else:
                    sp.dma_start(xin[p][:], x[i, k * P:(k + 1) * P, :]).then_inc(x_landed[p], 16)

            walk(sp, segs, load)
            sp.wait_ge(S["aux_set"], 5)
            for r in range(2):
                sp.dma_start(aux_d.rearrange("(b r) s k -> r b s k", r=2)[r], aux[:]).then_inc(S["aux_out"], 16)
            sp.wait_ge(S["aux_out"], 32)

        @block.gpsimd
        def _(pool):
            pool.memset(one[:], 1.0).then_inc(S["idx_set"], 1)
            pool.iota(idx_i[:, 0:TXT_FULL], pattern=[[P, TXT_FULL]], base=0, channel_multiplier=1).then_inc(S["idx_set"], 1)
            for r in range(2):
                pool.wait_ge(S["idx_set"], 2 + r)
                pool.iota(idx_i[r * REM:(r + 1) * REM, TXT_FULL:], pattern=[[1, 1]], base=TXT_FULL * P,
                          channel_multiplier=1).then_inc(S["idx_set"], 1)
            pool.wait_ge(S["idx_set"], 4)
            pool.iota(kidx_i[:], pattern=[[1, SK]], base=-NIMG, channel_multiplier=0).then_inc(S["idx_set"], 1)
            for rows_, keys_, value in ((slice(1, 3), slice(0, NIMG), 0.0), (slice(1, 3), slice(NIMG, SK), 1.0),
                                        (slice(3, 5), slice(0, NIMG), 1.0), (slice(3, 5), slice(NIMG, SK), 0.0)):
                pool.memset(aux[:, rows_, keys_], value).then_inc(S["aux_set"], 1)

        @block.tensor
        def _(pe):
            def turn(dst, src, done):
                for c in range(NG):
                    last = pe.transpose(dst[:, c * P:(c + 1) * P], src[:, c * P:(c + 1) * P], ident[:])
                last.then_inc(done, 1)

            def turn_x(p, n, half):
                pe.wait_ge(x_ready[p], 16 * (half + 1))
                if not (isinstance(n, int) and n < 2):
                    pe.wait_ge(S["xl_done"], n - 1)
                turn(psx[:, p, :], xin[p], S["tx_done"])

            def turn_k(t):
                pe.wait_ge(S["kn_done"], t.n + 1)
                if not (isinstance(t.n, int) and t.n < 2):
                    pe.wait_ge(S["kl_done"], t.n - 1)
                turn(pst[:, t.par, :], kn[t.par], S["tk_done"])

            def step(t):
                p, n = t.par, t.n
                if t.first:
                    turn_x(0, 0, 0)
                if not t.last:
                    turn_x(1 - p, n + 1, t.next_half)
                w = {"img": ("wki", "wvi"), "extra": ("wki", "wvi"), "txt": ("wk", "wv"), "rem": ("wk", "wv"), "q": ("wq", None)}[t.seg.kind]
                xc = lambda part: (lambda c: part[p][:, c * P:(c + 1) * P])
                wc = lambda part: (lambda c: part[:, c, :])
                pe.wait_ge(S["xl_done"], n + 1)
                if not (isinstance(n, int) and n < 2):
                    pe.wait_ge(S["kb_done"], n - 1)
                hi, lo = weights[w[0]]
                split_matmuls(nc, psk[:, p, :], xc(xh), xc(xl), wc(hi), wc(lo), NG).then_inc(S["mmk_done"], 1)
                if not t.first:
                    turn_k(t.prev())
                if w[1]:
                    if not (isinstance(n, int) and n < 2):
                        pe.wait_ge(S["v_done"], n - 1)
                    hi, lo = weights[w[1]]
                    last = split_matmuls(nc, psv[:, p, :], xc(xh), xc(xl), wc(hi), wc(lo), NG)
                    last.then_inc(S["mmv_done"], 1)

                if t.last:
                    turn_k(t)

            walk(pe, segs, step)

        @block.scalar
        def _(act):
            def high_x(p, n):
                act.wait_ge(S["tx_done"], n + 1)
                act.activation(xh[p][:], psx[:, p, :], ACT.Copy).then_inc(S["xh_done"], 1)

            def finish_k(t):
                p = t.par
                act.wait_ge(S["tk_done"], t.n + 1)
                if not (isinstance(t.n, int) and t.n < 2):
                    act.wait_ge(stored[p], t.stored_before)
                act.activation(kh[p][:], pst[:, p, :], ACT.Copy).then_inc(S["kh_done"], 1)

            def store(t):
                p, i, k, kind = t.par, t.i, t.k, t.seg.kind
                act.wait_ge(S["kl_done"], t.n + 1)
                h3, l3 = (b[p].bitcast(F32).rearrange("d (c t) -> d c t", c=NG) for b in (kh, kl))
                v3 = vs[p].rearrange("t (c d) -> t c d", c=NG)
                out = lambda dst, src, **how: act.dma_start(dst, src, **how).then_inc(stored[p], 16)
                if kind == "q":
                    out(qhv[i, :, :, k * P:(k + 1) * P].bitcast(F32), h3)
                    out(qlv[i, :, :, k * P:(k + 1) * P].bitcast(F32), l3)
                    return
                act.wait_ge(S["v_done"], t.n + 1)
                if kind == "extra":
                    for c in range(NG):
                        out(khv[:, :, c, NIMG - 1].rearrange("b d -> d b").bitcast(F32), h3[:, c, 0:B], allow_slow_non_contiguous=True)
                        out(klv[:, :, c, NIMG - 1].rearrange("b d -> d b").bitcast(F32), l3[:, c, 0:B], allow_slow_non_contiguous=True)
                    out(vv[:, NIMG - 1, :, :], v3[0:B])
                elif kind == "rem":
                    for r in range(2):
                        at = slice(r * REM, (r + 1) * REM)
                        out(khv[2 * k + r, :, :, SK - REM:SK].bitcast(F32), h3[:, :, at])
                        out(klv[2 * k + r, :, :, SK - REM:SK].bitcast(F32), l3[:, :, at])
                        out(vv[2 * k + r, SK - REM:SK, :, :], v3[at])
                else:
                    k0 = k * P + (NIMG if kind == "txt" else 0)
                    out(khv[i, :, :, k0:k0 + P].bitcast(F32), h3)
                    out(klv[i, :, :, k0:k0 + P].bitcast(F32), l3)
                    out(vv[i, k0:k0 + P, :, :], v3)

            def norm_sqrt(t_n, p):
                act.wait_ge(S["ln_step"], 7 * t_n + 3)
                act.activation(lcols[p][:, 5:6], lcols[p][:, 9:10], ACT.Sqrt, bias=0.0).then_inc(S["lnsq_done"], 1)

            def step(t):
                p, n = t.par, t.n
                if t.first:
                    high_x(0, 0)
                if not t.last:
                    if t.seg.kind == "q" or (t.seg.kind == "rem" and t.k == t.seg.T - 1):
                        norm_sqrt(n + 1 - Q0, 1 - p)
                    high_x(1 - p, n + 1)
                act.wait_ge(S["kb_done"], n + 1)
                act.activation(squares[:], kb[p][:], ACT.Square, accum_out=cols[p][:, 6:7]).then_inc(S["ss_done"], 1)
                act.wait_ge(S["ss_done"], n + 1)
                act.activation(cols[p][:, 5:6], cols[p][:, 6:7], ACT.Sqrt, scale=1.0 / D, bias=RMS_EPS).then_inc(S["sq_done"], 1)
                if not t.first:
                    finish_k(t.prev())
                if t.seg.kind != "q":
                    act.wait_ge(S["mmv_done"], n + 1)
                    if not (isinstance(n, int) and n < 2):
                        act.wait_ge(stored[p], t.stored_before)
                    act.activation(vs[p][:], psv[:, p, :], ACT.Copy).then_inc(S["v_done"], 1)
                if not t.first:
                    store(t.prev())
                if t.last:
                    finish_k(t)
                    store(t)
                    act.wait_ge(stored[p], t.stored)
                    act.wait_ge(stored[1 - p], t.prev().stored)
            walk(act, segs, step)

        @block.vector
        def _(dve):
            def norm_x(p, nq, half):
                L = lcols[p]
                dve.wait_ge(x_landed[p], 16 * (half + 1))
                r = layer_norm_rstd(dve, L, stats[p], xin[p], S["ln_step"], 7 * nq, S["lnsq_done"], nq + 1)
                dve.tensor_scalar(xin[p][:], xin[p][:], L[:, 6:7], r, ALU.subtract, ALU.mult).then_inc(x_ready[p], 16)

            def low_x(p, n):
                dve.wait_ge(S["xh_done"], n + 1)
                dve.tensor_tensor(xl[p][:], psx[:, p, :], xh[p][:].bitcast(F32), ALU.subtract).then_inc(S["xl_done"], 1)

            def low_k(t):
                p = t.par
                dve.wait_ge(S["kh_done"], t.n + 1)
                if not (isinstance(t.n, int) and t.n < 2):
                    dve.wait_ge(stored[p], t.stored_before)
                dve.tensor_tensor(kl[p][:], pst[:, p, :], kh[p][:].bitcast(F32), ALU.subtract).then_inc(S["kl_done"], 1)

            def step(t):
                p, n, kind = t.par, t.n, t.seg.kind
                if t.first:
                    low_x(0, 0)
                if not t.last:
                    if kind == "q":
                        norm_x(1 - p, n + 1 - Q0, t.i * (QT // 2) + (t.k + 1) // 2)
                    elif kind == "rem" and t.k == t.seg.T - 1:
                        norm_x(1 - p, 0, 0)
                    low_x(1 - p, n + 1)
                dve.wait_ge(S["mmk_done"], n + 1)
                dve.tensor_tensor(kb[p][:], psk[:, p, :], bias[g(kind)][:], ALU.add).then_inc(S["kb_done"], 1)
                dve.wait_ge(S["ss_done"], n + 1)
                live = one[:]
                if kind == "txt":
                    live = valid[:, bass.ds(t.i * TXT_FULL + t.k, 1)]
                elif kind == "rem":
                    live = validr[:, t.k:t.k + 1]
                r = rstd_steps(dve, cols[p], cols[p][:, 6:7], S["step"], 1.0 / D, RMS_EPS, S["sq_done"], n + 1, 5 * n, live)
                if not (isinstance(n, int) and n < 2):
                    dve.wait_ge(S["tk_done"], n - 1)
                dve.scalar_tensor_tensor(kn[p][:], kb[p][:], r, gain[g(kind)][:], ALU.mult, ALU.mult).then_inc(S["kn_done"], 1)
                if not t.first:
                    low_k(t.prev())
                if t.last:
                    low_k(t)

            dve.wait_ge(S["const_in"], 16 * 8)
            dve.wait_ge(S["idx_set"], 5)
            dve.tensor_copy(len_f[:], len_i[:]).then_inc(S["len_set"], 1)
            dve.tensor_copy(idx_f[:], idx_i[:]).then_inc(S["len_set"], 1)
            dve.tensor_copy(kidx_f[:], kidx_i[:]).then_inc(S["len_set"], 1)
            dve.tensor_scalar(klen_f[:], klen_i[:], 0.0, None, ALU.max).then_inc(S["len_set"], 1)
            dve.wait_ge(S["len_set"], 4)
            for b in range(B):
                dve.tensor_scalar(valid[:, b * TXT_FULL:(b + 1) * TXT_FULL], idx_f[:, 0:TXT_FULL], len_f[:, b:b + 1], None,
                                  ALU.is_lt).then_inc(S["valid_set"], 1)
            for r in range(2):
                at = slice(r * REM, (r + 1) * REM)
                dve.tensor_tensor(validr[at, :], idx_f[at, TXT_FULL:].to_broadcast([REM, B // 2]),
                                  len_f[at, :].rearrange("p (j r) -> p r j", r=2)[:, r, :], ALU.is_lt).then_inc(S["valid_set"], 1)
            dve.wait_ge(S["valid_set"], B + 2)
            dve.tensor_scalar(aux[:, 0, :], kidx_f[:], klen_f[:], -MASKED, ALU.is_ge, ALU.mult).then_inc(S["aux_set"], 1)
            walk(dve, segs, step)


def attend(nc, scratch, out_t, b_v, b_v_img):
    kh_d, kl_d, v_d, qh_d, ql_d, aux_d = scratch
    ROWS = 3 * HD
    STACK = ROWS + AUX
    CH = [(0, 512), (512, 512), (1024, 512), (1535, SK - 1535)]
    NCH = len(CH)
    NMAX = HG * QT * NCH
    NALL = NMAX + HG
    VLOADS = 5
    with ExitStack() as ctx:
        a = Names(nc, ctx, "at")
        kst = [a.sb(f"kst{p}", [STACK, HG, SK], F32R) for p in range(2)]
        qst = [a.sb(f"qst{p}", [STACK, HG, SQ], F32R) for p in range(2)]
        vt = [a.sb(f"vt{p}", [P, KT, P]) for p in range(2)]
        vmix = [a.sb(f"vmix{p}", [P, P]) for p in range(2)]
        probs = a.sb("probs", [P, 2, HG, SQ])
        ones = a.sb("ones", [P, HD])
        ones_img = a.sb("ones_img", [P, HD])
        ones_txt = a.sb("ones_txt", [P, HD])
        identb = a.sb("identb", [P, P], BF16)
        cm = a.sb("cm", [P, HG * QT, 4])
        top = a.sb("top", [P, HG * QT, 2])
        neg = a.sb("neg", [P, HG * QT, AUX], BF16)
        bv_in = a.sb("bv_in", [P, 2, GROUPS])
        bv = a.sb("bv", [P, GROUPS])
        rl = a.sb("rl", [P, 2, SQ])
        oi = a.sb("oi", [P, SQ])
        ot = a.sb("ot", [P, SQ])
        res = [a.sb(f"res{p}", [P, SQ]) for p in range(2)]
        st, mx, acc = a.banks("st", HG), a.banks("mx", 2), a.banks("acc", 2)
        k_in = [[a.sem(f"k_in{p}{h}") for h in range(HG)] for p in range(2)]
        q_in = [a.sem(f"q_in{p}") for p in range(2)]
        v_in = [a.sem(f"v_in{p}") for p in range(2)]
        saved = [a.sem(f"saved{p}") for p in range(2)]
        names = "const_set bv_set st_done exp_done pv_done mx_full mx_free neg_step top_copied img_full acc_free evac res_done const_dve".split()
        S = {n: a.sem(n) for n in names}
        block = ctx.enter_context(nc.Block())
        NC = 4 + 1 + 8

        plan = {}
        slots = [(t, h) for t in range(1, 11) for h in range(HG)]
        for m in range(NMAX):
            plan.setdefault(slots[m * len(slots) // NMAX], []).append(m)
        for j, at in enumerate([(11, 1), (11, 3), (12, 1), (12, 3)]):
            plan[at] = [NMAX + j]

        def chunk(m):
            return m // (QT * NCH), m // NCH % QT, m % NCH

        def pairs(eng, body):
            with eng.Fori(0, GROUPS // 2 - 1) as i:
                for par in range(2):
                    body(i, par, False)
            for par in range(2):
                body(GROUPS // 2 - 1, par, par == 1)

        def keys(t):
            return P if t < KT - 1 else KLAST

        @block.sync
        def _(sp):
            def load(G, p, pair):
                src_q = lambda d: d[G].bitcast(F32).rearrange("(h d) q -> d h q", d=HD)
                for r, d in enumerate((qh_d, ql_d, qh_d)):
                    sp.dma_start(qst[p][r * HD:(r + 1) * HD, :, :].bitcast(F32), src_q(d)).then_inc(q_in[p], 16)
                for h in range(HG):
                    for r, d in enumerate((kh_d, kh_d, kl_d)):
                        sp.dma_start(kst[p][r * HD:(r + 1) * HD, h, :].bitcast(F32),
                                     d[G, h * HD:(h + 1) * HD, :].bitcast(F32)).then_inc(k_in[p][h], 16)
                    sp.dma_start(kst[p][ROWS:STACK, h, :].bitcast(F32), aux_d[pair]).then_inc(k_in[p][h], 16)
                v = v_d[G]
                m0 = MIX * P
                sp.dma_start(vt[p][:, 0:MIX, :], v[0:m0, :].rearrange("(t k) d -> k t d", k=P)).then_inc(v_in[p], 16)
                sp.dma_start(vmix[p][0:1, :], v[m0:m0 + 1, :]).then_inc(v_in[p], 16)
                sp.dma_start(vt[p][1:P, MIX, :], v[m0 + 1:m0 + P, :]).then_inc(v_in[p], 16)
                sp.dma_start(vt[p][:, MIX + 1:KT - 1, :],
                             v[m0 + P:(KT - 1) * P, :].rearrange("(t k) d -> k t d", k=P)).then_inc(v_in[p], 16)
                sp.dma_start(vt[p][0:KLAST, KT - 1, :], v[(KT - 1) * P:SK, :]).then_inc(v_in[p], 16)

            for r, src in enumerate((b_v, b_v_img)):
                for c in range(NG):
                    for b in range(B):
                        sp.dma_start(bv_in[:, r, b * NG + c:b * NG + c + 1],
                                     src[c * P:(c + 1) * P].rearrange("(p o) -> p o", o=1),
                                     allow_slow_non_contiguous=True).then_inc(S["bv_set"], 16)
            sp.wait_ge(S["const_set"], NC)
            load(0, 0, 0)

            def body(i, par, last):
                G = 2 * i + par
                if not last:
                    sp.wait_ge(S["pv_done"], KT * G + 2)
                    load(G + 1, 1 - par, i if par == 0 else i + 1)
                sp.wait_ge(S["res_done"], G + 1)
                sp.dma_start(out_t[G], res[par][:]).then_inc(saved[par], 16)

            sp.sem_inc(saved[0], 16)
            sp.sem_inc(saved[1], 16)
            pairs(sp, body)
            for p in range(2):
                sp.wait_ge(saved[p], 16 * (GROUPS // 2 + 1))

        @block.gpsimd
        def _(pool):
            pool.memset(ones[:], 1.0).then_inc(S["const_set"], 1)
            pool.memset(ones_img[:], 0.0).then_inc(S["const_set"], 1)
            pool.memset(ones_txt[:], 1.0).then_inc(S["const_set"], 1)
            pool.memset(identb[:], 0.0).then_inc(S["const_set"], 1)
            pool.wait_ge(S["const_set"], 4)
            pool.affine_select(out=identb[:], in_=identb[:], compare_op=ALU.not_equal, fill=1.0, base=0,
                               pattern=[[-1, P]], channel_multiplier=1).then_inc(S["const_set"], 1)
            sets = [(vmix[p][:], 0.0) for p in range(2)] + [(ones_img[0:1, :], 1.0), (ones_txt[0:1, :], 0.0)]
            sets += [(vt[p][0:1, MIX, :], 0.0) for p in range(2)]
            sets += [(qst[p][ROWS:ROWS + 1, :, :].bitcast(F32), 1.0) for p in range(2)]
            for n, (where, value) in enumerate(sets):
                pool.wait_ge(S["const_set"], 5 + n)
                pool.memset(where, value).then_inc(S["const_set"], 1)

        @block.tensor
        def _(pe):
            def maxima(W, i, p, m):
                slot = m % 2
                if m < NMAX:
                    h, qt, kc = chunk(m)
                    k0, kn = CH[kc]
                    if m == 0:
                        pe.wait_ge(q_in[p], 48 * (i + 1))
                    if m % (QT * NCH) == 0:
                        pe.wait_ge(k_in[p][h], 64 * (i + 1))
                    if m >= 2:
                        pe.wait_ge(S["mx_free"], NMAX * W + m - 1)
                    elif not (isinstance(W, int) and W == 0):
                        pe.wait_ge(S["top_copied"], HG * (W - 1) + 3 + m)
                    pe.matmul(mx[:, slot, 0:kn], qst[p][0:ROWS + 1, h, qt * P:(qt + 1) * P],
                              kst[p][0:ROWS + 1, h, k0:k0 + kn], start=True, stop=True).then_inc(S["mx_full"], 1)
                    return
                h = m - NMAX
                if h == 0:
                    pe.wait_ge(S["neg_step"], 3 * (W + 1))
                if h < 2:
                    pe.wait_ge(S["mx_free"], NMAX * W + m - 1)
                else:
                    pe.wait_ge(S["top_copied"], HG * W + h - 1)
                for qt in range(QT):
                    last = pe.matmul(mx[ROWS:STACK, slot, qt * P:(qt + 1) * P], neg[:, h * QT + qt, :], identb[:],
                                     start=True, stop=True)
                last.then_inc(S["mx_full"], 1)

            def values(G, i, p, t):
                n, kn = KT * G + t, keys(t)
                pe.wait_ge(S["exp_done"], HG * (n + 1) + HG)
                if t == 0:
                    pe.wait_ge(v_in[p], 16 * VLOADS * (i + 1))
                runs = []
                if t <= MIX:
                    runs.append((vmix[p] if t == MIX else None, ones_img if t == MIX else ones, t == 0, t == MIX))
                if t >= MIX:
                    runs.append((None, ones_txt if t == MIX else ones, t == MIX, t == KT - 1))
                for r, (mixed, one, first, end) in enumerate(runs):
                    if first:
                        pe.wait_ge(S["acc_free"], 2 * G + (2 if t == MIX else 1))
                    for h in range(HG):
                        cols = slice(h * HD, (h + 1) * HD)
                        v = mixed[0:kn, cols] if mixed is not None else vt[p][0:kn, t, cols]
                        pe.matmul(acc[cols, 0, :], v, probs[0:kn, (p + t) % 2, h, :], start=first, stop=end)
                    for h in range(HG):
                        cols = slice(h * HD, (h + 1) * HD)
                        last = pe.matmul(acc[cols, 1, :], one[0:kn, :], probs[0:kn, (p + t) % 2, h, :], start=first, stop=end)
                    last.then_inc(S["img_full"] if r < len(runs) - 1 else S["pv_done"], 1)

            def body(i, par, last):
                G = 2 * i + par
                Wi = i if par == 0 else i + 1
                for t in range(KT):
                    kn = keys(t)
                    for h in range(HG):
                        n = KT * G + t
                        if t == 0:
                            pe.wait_ge(S["top_copied"], HG * G + h + 1)
                        pe.wait_ge(S["exp_done"], HG * n + h + 1)
                        pe.matmul(st[0:kn, h, :], kst[par][:, h, t * P:t * P + kn], qst[par][:, h, :],
                                  start=True, stop=True).then_inc(S["st_done"], 1)
                        if not last:
                            for m in plan.get((t, h), []):
                                maxima(G + 1, Wi, 1 - par, m)
                    if t >= 1:
                        values(G, i, par, t - 1)
                values(G, i, par, KT - 1)

            pe.wait_ge(S["const_set"], NC)
            for m in range(NALL):
                maxima(0, 0, 0, m)
            pairs(pe, body)

        @block.scalar
        def _(act):
            def copy_top(W, p, j):
                act.wait_ge(S["mx_full"], NALL * W + NMAX + j + 1)
                act.activation(qst[p][ROWS:STACK, j, :], mx[ROWS:STACK, (NMAX + j) % 2, :], ACT.Copy).then_inc(S["top_copied"], 1)

            def body(i, par, last):
                G = 2 * i + par
                for t in range(KT):
                    kn = keys(t)
                    for h in range(HG):
                        n = KT * G + t
                        act.wait_ge(S["st_done"], HG * n + h + 1)
                        if h == 0:
                            act.wait_ge(S["pv_done"], n + 1)
                        act.activation(probs[0:kn, (par + t) % 2, h, :], st[0:kn, h, :], ACT.Exp,
                                       scale=SCALE).then_inc(S["exp_done"], 1)
                        if not last:
                            for m in plan.get((t, h), []):
                                if m >= NMAX:
                                    copy_top(G + 1, 1 - par, m - NMAX)

            act.sem_inc(S["exp_done"], HG)
            act.sem_inc(S["pv_done"], 2)
            act.wait_ge(S["const_set"], NC)
            for j in range(HG):
                copy_top(0, 0, j)
            pairs(act, body)

        @block.vector
        def _(dve):
            def reduce(W, m):
                h, qt, kc = chunk(m)
                col, slot = h * QT + qt, m % 2
                dve.wait_ge(S["mx_full"], NALL * W + m + 1)
                if kc == 0:
                    dve.reduce_max(top[:, col, 1:2], mx[:, slot, 0:NIMG], AX.X)
                    dve.reduce_max(cm[:, col, 0:1], mx[:, slot, NIMG:512], AX.X).then_inc(S["mx_free"], 1)
                else:
                    dve.reduce_max(cm[:, col, kc:kc + 1], mx[:, slot, 0:CH[kc][1]], AX.X).then_inc(S["mx_free"], 1)

            def negate(W):
                dve.wait_ge(S["mx_free"], NMAX * (W + 1))
                if not (isinstance(W, int) and W == 0):
                    dve.wait_ge(S["mx_full"], NALL * W)
                dve.tensor_reduce(top[:, :, 0:1], cm[:], AX.X, ALU.max).then_inc(S["neg_step"], 1)
                dve.wait_ge(S["neg_step"], 3 * W + 1)
                nv = neg[:, :, 1:5].rearrange("p c (k s) -> p c k s", s=2)
                dve.tensor_scalar(nv[:, :, :, 0], top[:], -1.0, None, ALU.mult).then_inc(S["neg_step"], 1)
                dve.wait_ge(S["neg_step"], 3 * W + 2)
                dve.scalar_tensor_tensor(nv[:, :, :, 1], top[:], -1.0, nv[:, :, :, 0], ALU.mult, ALU.subtract).then_inc(S["neg_step"], 1)

            def evac_img(G):
                dve.wait_ge(S["img_full"], G + 1)
                dve.reciprocal(rl[:, 0, :], acc[:, 1, :]).then_inc(S["evac"], 1)
                dve.wait_ge(S["evac"], 2 * G + 1)
                dve.tensor_tensor(oi[:], acc[:, 0, :], rl[:, 0, :], ALU.mult).then_inc(S["acc_free"], 1)

            def evac_txt(G, i, par):
                dve.wait_ge(S["pv_done"], KT * (G + 1) + 2)
                dve.reciprocal(rl[:, 1, :], acc[:, 1, :]).then_inc(S["evac"], 1)
                dve.wait_ge(S["evac"], 2 * G + 2)
                dve.tensor_tensor(ot[:], acc[:, 0, :], rl[:, 1, :], ALU.mult).then_inc(S["acc_free"], 1)
                dve.wait_ge(S["acc_free"], 2 * G + 3)
                dve.wait_ge(saved[par], 16 * (i + 1))
                dve.scalar_tensor_tensor(res[par][:], ot[:], bv[:, bass.ds(G, 1)], oi[:], ALU.add, ALU.add).then_inc(S["res_done"], 1)

            def body(i, par, last):
                G = 2 * i + par
                for t in range(KT):
                    for h in range(HG):
                        if not last:
                            for m in plan.get((t, h), []):
                                if m < NMAX:
                                    reduce(G + 1, m)
                                if m == NMAX - 1:
                                    negate(G + 1)
                    if t == MIX + 1:
                        evac_img(G)
                evac_txt(G, i, par)

            dve.sem_inc(S["acc_free"], 1)
            dve.memset(neg[:], 1.0).then_inc(S["const_dve"], 1)
            dve.wait_ge(S["const_dve"], 1)
            dve.wait_ge(S["bv_set"], 16 * 2 * GROUPS)
            dve.tensor_tensor(bv[:], bv_in[:, 0, :], bv_in[:, 1, :], ALU.add).then_inc(S["const_dve"], 1)
            dve.wait_ge(S["const_dve"], 2)
            for m in range(NMAX):
                reduce(0, m)
            negate(0)
            pairs(dve, body)


def residual(nc, ident, x, out_t, wo, b_o, g_xattn, x2_d, nh_d, nl_d):
    segs = [Seg("o", B, QT, 3)]
    otv = out_t.rearrange("(b c) d q -> b d c q", c=NG)
    with ExitStack() as ctx:
        a = Names(nc, ctx, "rs")
        two = lambda name, shape, dt=F32: [a.sb(f"{name}{p}", shape, dt) for p in range(2)]
        oin, xin, scaled, x2, xn = (two(n, [P, D]) for n in ("oin", "xin", "scaled", "x2", "xn"))
        oh, ol, nh, nl = (two(n, [P, D], F32R) for n in ("oh", "ol", "nh", "nl"))
        L, stats = two("cols", [P, 16]), two("stats", [P, 6])
        gate, gate_in, bo, gated_bo = a.sb("gate", [P, 1]), a.sb("gate_in", [P, 1]), a.sb("bo", [P, D]), a.sb("gated_bo", [P, D])
        pso, psn = a.banks("pso", 2), a.banks("psn", 2)
        landed = [a.sem(f"landed{p}") for p in range(2)]
        stored = [a.sem(f"stored{p}") for p in range(2)]
        names = "const_in gate_done bo_done oh_done ol_done mm_done scaled_done x2_done step sq_done xn_done turned nh_done nl_done".split()
        S = {n: a.sem(n) for n in names}
        block = ctx.enter_context(nc.Block())
        early = lambda n: isinstance(n, int) and n < 2

        @block.sync
        def _(sp):
            sp.dma_start(gate_in[:], g_xattn.partition_broadcast(P)).then_inc(S["const_in"], 16)
            sp.dma_start(bo[:], b_o.partition_broadcast(P)).then_inc(S["const_in"], 16)

            def load(t):
                p = t.par
                if not early(t.n):
                    sp.wait_ge(S["ol_done"], t.n - 1)
                    sp.wait_ge(S["scaled_done"], t.n - 1)
                rows = slice(t.k * P, (t.k + 1) * P)
                sp.dma_start(oin[p].rearrange("d (c q) -> d c q", c=NG), otv[t.i, :, :, rows]).then_inc(landed[p], 16)
                sp.dma_start(xin[p][:], x[t.i, rows, :]).then_inc(landed[p], 16)

            walk(sp, segs, load)

        @block.tensor
        def _(pe):
            def turn(t):
                p = t.par
                pe.wait_ge(S["xn_done"], t.n + 1)
                if not early(t.n):
                    pe.wait_ge(S["nl_done"], t.n - 1)
                for c in range(NG):
                    last = pe.transpose(psn[:, p, c * P:(c + 1) * P], xn[p][:, c * P:(c + 1) * P], ident[:])
                last.then_inc(S["turned"], 1)

            def step(t):
                p = t.par
                pe.wait_ge(S["ol_done"], t.n + 1)
                if not early(t.n):
                    pe.wait_ge(S["scaled_done"], t.n - 1)
                oc = lambda part: (lambda c: part[p][:, c * P:(c + 1) * P])
                wc = lambda part: (lambda c: part[:, c, :])
                split_matmuls(nc, pso[:, p, :], oc(oh), oc(ol), wc(wo[0]), wc(wo[1]), NG).then_inc(S["mm_done"], 1)
                if not t.first:
                    turn(t.prev())
                if t.last:
                    turn(t)

            walk(pe, segs, step)

        @block.scalar
        def _(act):
            def high_o(p, n, half):
                act.wait_ge(landed[p], 32 * (half + 1))
                if not early(n):
                    act.wait_ge(S["mm_done"], n - 1)
                act.activation(oh[p][:], oin[p][:], ACT.Copy).then_inc(S["oh_done"], 1)

            def finish(t):
                p = t.par
                act.wait_ge(S["turned"], t.n + 1)
                if not early(t.n):
                    act.wait_ge(stored[p], t.stored_before)
                act.activation(nh[p][:], psn[:, p, :], ACT.Copy).then_inc(S["nh_done"], 1)

            def store(t):
                p, rows = t.par, slice(t.k * P, (t.k + 1) * P)
                act.dma_start(x2_d[t.i, rows, :], x2[p][:]).then_inc(stored[p], 16)
                act.wait_ge(S["nl_done"], t.n + 1)
                for part, dst in ((nh, nh_d), (nl, nl_d)):
                    act.dma_start(dst[t.i, :, :, rows].bitcast(F32),
                                  part[p].bitcast(F32).rearrange("d (c q) -> d c q", c=NG)).then_inc(stored[p], 16)

            def step(t):
                p, n = t.par, t.n
                if t.first:
                    high_o(0, 0, 0)
                if not t.last:
                    high_o(1 - p, n + 1, t.next_half)
                act.wait_ge(S["step"], 7 * n + 3)
                act.activation(L[p][:, 5:6], L[p][:, 9:10], ACT.Sqrt, bias=0.0).then_inc(S["sq_done"], 1)
                if not t.first:
                    finish(t.prev())
                    store(t.prev())
                if t.last:
                    finish(t)
                    store(t)
                    act.wait_ge(stored[p], t.stored)
                    act.wait_ge(stored[1 - p], t.prev().stored)

            act.wait_ge(S["const_in"], 32)
            act.activation(gate[:], gate_in[:], ACT.Tanh).then_inc(S["gate_done"], 1)
            walk(act, segs, step)

        @block.vector
        def _(dve):
            def low_o(p, n):
                dve.wait_ge(S["oh_done"], n + 1)
                dve.tensor_tensor(ol[p][:], oin[p][:], oh[p][:].bitcast(F32), ALU.subtract).then_inc(S["ol_done"], 1)

            def low_n(t):
                p = t.par
                dve.wait_ge(S["nh_done"], t.n + 1)
                dve.tensor_tensor(nl[p][:], psn[:, p, :], nh[p][:].bitcast(F32), ALU.subtract).then_inc(S["nl_done"], 1)

            def step(t):
                p, n = t.par, t.n
                if t.first:
                    low_o(0, 0)
                if not t.last:
                    low_o(1 - p, n + 1)
                dve.wait_ge(S["mm_done"], n + 1)
                dve.scalar_tensor_tensor(scaled[p][:], pso[:, p, :], gate[:], xin[p][:], ALU.mult, ALU.add).then_inc(S["scaled_done"], 1)
                if not early(n):
                    dve.wait_ge(stored[p], t.stored_before)
                dve.wait_ge(S["scaled_done"], n + 1)
                dve.tensor_tensor(x2[p][:], scaled[p][:], gated_bo[:], ALU.add).then_inc(S["x2_done"], 1)
                dve.wait_ge(S["x2_done"], n + 1)
                c = layer_norm_rstd(dve, L[p], stats[p], x2[p], S["step"], 7 * n, S["sq_done"], n + 1)
                if not early(n):
                    dve.wait_ge(S["turned"], n - 1)
                dve.tensor_scalar(xn[p][:], x2[p][:], L[p][:, 6:7], c, ALU.subtract, ALU.mult).then_inc(S["xn_done"], 1)
                if not t.first:
                    low_n(t.prev())
                if t.last:
                    low_n(t)

            dve.wait_ge(S["gate_done"], 1)
            dve.tensor_scalar(gated_bo[:], bo[:], gate[:], None, ALU.mult).then_inc(S["bo_done"], 1)
            dve.wait_ge(S["bo_done"], 1)
            walk(dve, segs, step)


def layer_norm_rstd(dve, L, stats, src, step, base, sq_done, sq_value):
    dve.bn_stats(stats[:], src[:]).then_inc(step, 1)
    dve.wait_ge(step, base + 1)
    dve.tensor_copy(L[:, 10:11], stats[:, 0:1])
    dve.bn_aggr(L[:, 6:8], stats[:]).then_inc(step, 1)
    dve.wait_ge(step, base + 2)
    dve.tensor_scalar(L[:, 9:10], L[:, 7:8], LN_EPS, None, ALU.add).then_inc(step, 1)
    dve.wait_ge(step, base + 3)
    dve.wait_ge(sq_done, sq_value)
    dve.reciprocal(L[:, 1:2], L[:, 5:6]).then_inc(step, 1)
    dve.wait_ge(step, base + 4)
    dve.scalar_tensor_tensor(L[:, 2:3], L[:, 1:2], L[:, 1:2], L[:, 9:10], ALU.mult, ALU.mult).then_inc(step, 1)
    dve.wait_ge(step, base + 5)
    dve.tensor_scalar(L[:, 3:4], L[:, 2:3], -0.5, 1.5, ALU.mult, ALU.add).then_inc(step, 1)
    dve.wait_ge(step, base + 6)
    dve.tensor_scalar(L[:, 4:5], L[:, 3:4], L[:, 1:2], None, ALU.mult).then_inc(step, 1)
    dve.wait_ge(step, base + 7)
    return L[:, 4:5]


def ternarize(nc, w1, w2, t1, t2, alpha):
    NT = 16
    with ExitStack() as ctx:
        a = Names(nc, ctx, "tw")
        nat = [a.sb(f"nat{w}", [P, NT, D]) for w in range(2)]
        below = a.sb("below", [P, 2, D], BF16)
        prod = a.sb("prod", [P, 2, D])
        tern = [a.sb(f"tern{w}", [P, NT, D], BF16) for w in range(2)]
        identb = a.sb("identb", [P, P], BF16)
        top = a.sb("top", [P, 2, NT])
        m = a.sb("m", [P, 2, 8])
        sums = a.sb("sums", [P, 2, 3, NT])
        part = a.sb("part", [P, 2, 3])
        total = a.sb("total", [P, 2, 3])
        ps = a.banks("ps", 8)
        names = "ident_set rowmax allmax step t_done sum_done summed turned evac0 evac1 a_step".split()
        S = {n: a.sem(n) for n in names}
        w_in = [a.sem(f"w_in{w}") for w in range(2)]
        block = ctx.enter_context(nc.Block())
        srcs = (w1.rearrange("(t p) i -> p t i", p=P), w2.rearrange("(o p) (s i) -> p o s i", p=P, i=D))

        def bank(n, half):
            return ps[:, n % 8, half * 256:(half + 1) * 256].bitcast(BF16)

        def dst(n, half):
            j = 2 * n + half
            if j < 16:
                return t1[:, j // 4, (j % 4) * D:(j % 4 + 1) * D]
            return t2[:, j - 16, :]

        @block.sync
        def _(sp):
            sp.dma_start(nat[0][:], srcs[0]).then_inc(w_in[0], 16)
            sp.dma_start(nat[1][:].rearrange("p (o s) i -> p o s i", o=NG), srcs[1]).then_inc(w_in[1], 16)

        @block.gpsimd
        def _(pool):
            pool.memset(identb[:], 0.0).then_inc(S["ident_set"], 1)
            pool.wait_ge(S["ident_set"], 1)
            pool.affine_select(out=identb[:], in_=identb[:], compare_op=ALU.not_equal, fill=1.0, base=0,
                               pattern=[[-1, P]], channel_multiplier=1).then_inc(S["ident_set"], 1)
            for w in range(2):
                pool.wait_ge(S["rowmax"], 2 * (w + 1))
                pool.partition_all_reduce(m[:, w, 1:2], m[:, w, 0:1], P, RMAX).then_inc(S["allmax"], 1)
            for w in range(2):
                pool.wait_ge(S["sum_done"], w + 1)
                pool.partition_all_reduce(total[:, w, :], part[:, w, :], P, RADD).then_inc(S["summed"], 1)

        @block.vector
        def _(dve):
            for w in range(2):
                dve.wait_ge(w_in[w], 16)
                dve.tensor_reduce(top[:, w, :], nat[w][:], AX.X, ALU.max, apply_absolute_value=True).then_inc(S["rowmax"], 1)
                dve.wait_ge(S["rowmax"], 2 * w + 1)
                dve.reduce_max(m[:, w, 0:1], top[:, w, :], AX.X).then_inc(S["rowmax"], 1)
            for w in range(2):
                dve.wait_ge(S["allmax"], w + 1)
                dve.tensor_scalar(m[:, w, 2:3], m[:, w, 1:2], THRESHOLD, None, ALU.mult).then_inc(S["step"], 1)
                dve.tensor_scalar(m[:, w, 3:4], m[:, w, 1:2], -THRESHOLD, None, ALU.mult).then_inc(S["step"], 1)
                dve.wait_ge(S["step"], 2 * w + 2)
                for t in range(NT):
                    n = w * NT + t
                    if t >= 2:
                        dve.wait_ge(S["t_done"], 3 * (n - 1))
                    dve.tensor_scalar(below[:, t % 2, :], nat[w][:, t, :], m[:, w, 3:4], 0.0, ALU.is_lt, ALU.add,
                                      accum_out=sums[:, w, 0, t:t + 1]).then_inc(S["t_done"], 1)
                    dve.wait_ge(S["t_done"], 3 * n + 1)
                    dve.scalar_tensor_tensor(tern[w][:, t, :], nat[w][:, t, :], m[:, w, 2:3], below[:, t % 2, :], ALU.is_gt,
                                             ALU.subtract, accum_out=sums[:, w, 1, t:t + 1]).then_inc(S["t_done"], 1)
                    dve.wait_ge(S["t_done"], 3 * n + 2)
                    dve.scalar_tensor_tensor(prod[:, t % 2, :], tern[w][:, t, :], 1.0, nat[w][:, t, :], ALU.mult, ALU.mult,
                                             accum_out=sums[:, w, 2, t:t + 1]).then_inc(S["t_done"], 1)
                dve.wait_ge(S["t_done"], 3 * NT * (w + 1))
                dve.tensor_reduce(part[:, w, :], sums[:, w, :, :], AX.X, ALU.add).then_inc(S["sum_done"], 1)
            for w in range(2):
                b = 4 * w
                dve.wait_ge(S["summed"], w + 1)
                dve.scalar_tensor_tensor(m[:, w, 4:5], total[:, w, 0:1], 2.0, total[:, w, 1:2], ALU.mult, ALU.add).then_inc(S["a_step"], 1)
                dve.wait_ge(S["a_step"], b + 1)
                dve.tensor_scalar(m[:, w, 5:6], m[:, w, 4:5], 1.0, None, ALU.max).then_inc(S["a_step"], 1)
                dve.wait_ge(S["a_step"], b + 2)
                dve.reciprocal(m[:, w, 6:7], m[:, w, 5:6]).then_inc(S["a_step"], 1)
                dve.wait_ge(S["a_step"], b + 3)
                dve.tensor_tensor(alpha[:, w:w + 1], total[:, w, 2:3], m[:, w, 6:7], ALU.mult).then_inc(S["a_step"], 1)
            for n in range(8, 16):
                dve.wait_ge(S["turned"], n + 1)
                for half in range(2):
                    last = dve.tensor_copy(dst(n, half), bank(n, half))
                last.then_inc(S["evac1"], 1)

        @block.tensor
        def _(pe):
            pe.wait_ge(S["ident_set"], 2)
            for n in range(16):
                if n >= 8:
                    pe.wait_ge(S["evac0"], n - 7)
                for half in range(2):
                    j = 2 * n + half
                    for q in range(4):
                        if j < 16:
                            c, tile = j // 4, (j % 4) * 4 + q
                            pe.wait_ge(S["t_done"], 3 * tile + 2)
                            src = tern[0][:, tile, c * P:(c + 1) * P]
                        else:
                            f = j - 16
                            tile = q * 4 + f // 4
                            pe.wait_ge(S["t_done"], 3 * (16 + tile) + 2)
                            src = tern[1][:, tile, (f % 4) * P:(f % 4 + 1) * P]
                        last = pe.transpose(bank(n, half)[:, q * P:(q + 1) * P], src, identb[:])
                last.then_inc(S["turned"], 1)

        @block.scalar
        def _(act):
            for n in range(8):
                act.wait_ge(S["turned"], n + 1)
                for half in range(2):
                    last = act.activation(dst(n, half), bank(n, half), ACT.Copy)
                last.then_inc(S["evac0"], 1)


def feed_forward(nc, nh_d, nl_d, t1, t2, alpha, b1, b2, y_all, y_top):
    segs = [Seg("f", B // 2, 2, 0)]
    RING = 4
    with ExitStack() as ctx:
        a = Names(nc, ctx, "ff")
        xh = [a.sb(f"xh{p}", [P, NG, SQ], F32R) for p in range(2)]
        xl = [a.sb(f"xl{p}", [P, NG, SQ], F32R) for p in range(2)]
        h = a.sb("h", [P, RING, SQ])
        hh, hl = (a.sb(n, [P, RING, SQ], F32R) for n in ("hh", "hl"))
        b1c, b2r = a.sb("b1c", [P, NF]), a.sb("b2r", [P, D])
        psa, psy = a.banks("psa", RING), a.banks("psy", QT)
        x_in = [a.sem(f"x_in{p}") for p in range(2)]
        names = "const_in up_done gelu_done hh_done hl_done down_done y_done y_topped".split()
        S = {n: a.sem(n) for n in names}
        block = ctx.enter_context(nc.Block())
        early = lambda n, m: isinstance(n, int) and n < m

        @block.sync
        def _(sp):
            def load(t):
                if not early(t.n, 2):
                    sp.wait_ge(S["up_done"], NF * (t.n - 1))
                sp.dma_start(xh[t.par][:].bitcast(F32), nh_d[2 * t.i + t.k].bitcast(F32)).then_inc(x_in[t.par], 16)
                sp.dma_start(xl[t.par][:].bitcast(F32), nl_d[2 * t.i + t.k].bitcast(F32)).then_inc(x_in[t.par], 16)

            sp.dma_start(b1c[:], b1.rearrange("(f p) -> p f", p=P), allow_slow_non_contiguous=True).then_inc(S["const_in"], 16)
            sp.dma_start(b2r[:], b2.partition_broadcast(P)).then_inc(S["const_in"], 16)
            walk(sp, segs, load)

        @block.tensor
        def _(pe):
            def step(t):
                p, n = t.par, t.n

                def down(f):
                    r, N = f % RING, NF * n + f
                    pe.wait_ge(S["hl_done"], N + 1)
                    if f == 0 and not early(n, 1):
                        pe.wait_ge(S["y_done"], QT * n)
                    for j, part in enumerate((hh, hl)):
                        for q in range(QT):
                            last = pe.matmul(psy[:, q, :], part[:, r, q * P:(q + 1) * P], t2[:, f, :],
                                             start=(f == 0 and j == 0), stop=(f == NF - 1 and j == 1))
                    last.then_inc(S["down_done"], 1)

                pe.wait_ge(x_in[p], 32 * (t.half + 1))
                for f in range(NF):
                    r, N = f % RING, NF * n + f
                    if not early(N, RING):
                        pe.wait_ge(S["gelu_done"], N - RING + 1)
                    for c in range(NG):
                        for j, part in enumerate((xh, xl)):
                            last = pe.matmul(psa[:, r, :], t1[:, c, f * P:(f + 1) * P], part[p][:, c, :],
                                             start=(c == 0 and j == 0), stop=(c == NG - 1 and j == 1))
                    last.then_inc(S["up_done"], 1)
                    if f >= 2:
                        down(f - 2)
                down(NF - 2)
                down(NF - 1)

            walk(pe, segs, step)

        @block.scalar
        def _(act):
            def step(t):
                for f in range(NF):
                    r, N = f % RING, NF * t.n + f
                    act.wait_ge(S["up_done"], N + 1)
                    if not early(N, RING):
                        act.wait_ge(S["hl_done"], N - RING + 1)
                    act.activation(h[:, r, :], psa[:, r, :], ACT.Gelu, bias=b1c[:, f:f + 1], scale=alpha[:, 0:1]).then_inc(S["gelu_done"], 1)

            act.wait_ge(S["const_in"], 32)
            walk(act, segs, step)

        @block.vector
        def _(dve):
            def step(t):
                n = t.n
                for f in range(NF):
                    r, N = f % RING, NF * n + f
                    dve.wait_ge(S["gelu_done"], N + 1)
                    if not early(N, RING):
                        dve.wait_ge(S["down_done"], N - RING + 1)
                    dve.tensor_copy(hh[:, r, :], h[:, r, :]).then_inc(S["hh_done"], 1)
                    dve.wait_ge(S["hh_done"], N + 1)
                    dve.tensor_tensor(hl[:, r, :], h[:, r, :], hh[:, r, :].bitcast(F32), ALU.subtract).then_inc(S["hl_done"], 1)
                dve.wait_ge(S["down_done"], NF * (n + 1))
                for q in range(QT):
                    dve.scalar_tensor_tensor(y_all[:, bass.ds(QT * n + q, 1), :], psy[:, q:q + 1, :], alpha[:, 1:2],
                                             b2r[:].rearrange("p (o d) -> p o d", o=1), ALU.mult, ALU.add).then_inc(S["y_done"], 1)
                dve.wait_ge(S["y_done"], QT * (n + 1))
                dve.tensor_reduce(y_top[:, bass.ds(QT * n, QT)], y_all[:, bass.ds(QT * n, QT), :], AX.X, ALU.max,
                                  apply_absolute_value=True).then_inc(S["y_topped"], 1)

            dve.wait_ge(S["const_in"], 32)
            walk(dve, segs, step)
            dve.wait_ge(S["y_topped"], B)


def quantize(nc, x2_d, y_all, y_top, g_ffn, out):
    segs = [Seg("z", B // 2, 2, 1)]
    with ExitStack() as ctx:
        a = Names(nc, ctx, "qz")
        x2 = [a.sb(f"x2{p}", [P, QT, D]) for p in range(2)]
        level = [a.sb(f"level{p}", [P, QT, D]) for p in range(2)]
        res = [a.sb(f"res{p}", [P, QT, D]) for p in range(2)]
        gate_in, gate = a.sb("gate_in", [P, 1]), a.sb("gate", [P, 1])
        c = a.sb("c", [P, 8])
        landed = [a.sem(f"landed{p}") for p in range(2)]
        stored = [a.sem(f"stored{p}") for p in range(2)]
        names = "gate_in_s gate_done rowmax allmax step rounded clipped level_done res_done".split()
        S = {n: a.sem(n) for n in names}
        block = ctx.enter_context(nc.Block())
        early = lambda n: isinstance(n, int) and n < 2
        rows = lambda d, t: d[2 * t.i + t.k].rearrange("(q p) d -> p q d", p=P)
        mine = lambda t: y_all[:, bass.ds(QT * t.n, QT), :]

        @block.sync
        def _(sp):
            sp.dma_start(gate_in[:], g_ffn.partition_broadcast(P)).then_inc(S["gate_in_s"], 16)

            def load(t):
                if not early(t.n):
                    sp.wait_ge(S["res_done"], t.n - 1)
                sp.dma_start(x2[t.par][:], rows(x2_d, t)).then_inc(landed[t.par], 16)

            walk(sp, segs, load)

        @block.gpsimd
        def _(pool):
            pool.wait_ge(S["rowmax"], 1)
            pool.partition_all_reduce(c[:, 1:2], c[:, 0:1], P, RMAX).then_inc(S["allmax"], 1)

        @block.scalar
        def _(act):
            def store(t):
                act.wait_ge(S["res_done"], t.n + 1)
                act.dma_start(rows(out, t), res[t.par][:]).then_inc(stored[t.par], 16)

            def step(t):
                act.wait_ge(S["clipped"], t.n + 1)
                if not early(t.n):
                    act.wait_ge(S["res_done"], t.n - 1)
                act.activation(level[t.par][:], mine(t), ACT.Copy, bias=-MAGIC).then_inc(S["level_done"], 1)
                if not t.first:
                    store(t.prev())
                if t.last:
                    store(t)
                    act.wait_ge(stored[t.par], t.stored)
                    act.wait_ge(stored[1 - t.par], t.prev().stored)

            act.wait_ge(S["gate_in_s"], 16)
            act.activation(gate[:], gate_in[:], ACT.Tanh).then_inc(S["gate_done"], 1)
            walk(act, segs, step)

        @block.vector
        def _(dve):
            def clip(t):
                dve.tensor_scalar(mine(t), mine(t), c[:, 4:5], MAGIC, ALU.mult, ALU.add).then_inc(S["rounded"], 1)
                dve.wait_ge(S["rounded"], t.n + 1)
                dve.tensor_scalar(mine(t), mine(t), MAGIC + QMAX, MAGIC - QMAX, ALU.min, ALU.max).then_inc(S["clipped"], 1)

            def add(t):
                p = t.par
                dve.wait_ge(S["level_done"], t.n + 1)
                dve.wait_ge(landed[p], 16 * (t.half + 1))
                if not early(t.n):
                    dve.wait_ge(stored[p], t.stored_before)
                dve.scalar_tensor_tensor(res[p][:], level[p][:], c[:, 5:6], x2[p][:], ALU.mult, ALU.add).then_inc(S["res_done"], 1)

            def step(t):
                clip(t)
                if not t.first:
                    add(t.prev())
                if t.last:
                    add(t)

            dve.reduce_max(c[:, 0:1], y_top[:], AX.X).then_inc(S["rowmax"], 1)
            dve.wait_ge(S["allmax"], 1)
            dve.tensor_scalar(c[:, 2:3], c[:, 1:2], 1.0 / QMAX, ACT_EPS, ALU.mult, ALU.add).then_inc(S["step"], 1)
            dve.wait_ge(S["step"], 1)
            dve.wait_ge(S["gate_done"], 1)
            dve.reciprocal(c[:, 4:5], c[:, 2:3]).then_inc(S["step"], 1)
            dve.tensor_tensor(c[:, 5:6], c[:, 2:3], gate[:], ALU.mult).then_inc(S["step"], 1)
            dve.wait_ge(S["step"], 3)
            walk(dve, segs, step)


def flamingo_block(nc, x, ctx_in, lens, g_xattn, g_ffn, w_q, b_q, w_k, b_k, w_v, b_v, w_k_img, b_k_img, w_v_img, b_v_img,
                   w_o, b_o, g_q, g_k, g_k_img, w1, b1, w2, b2, out):
    dram = lambda name, shape, dt: nc.dram_tensor(name, shape, dt).ap()
    kh_d, kl_d = (dram(n, [GROUPS, P, SK], F32R) for n in ("k_high", "k_low"))
    qh_d, ql_d = (dram(n, [GROUPS, P, SQ], F32R) for n in ("q_high", "q_low"))
    v_d = dram("values", [GROUPS, SK, P], F32)
    aux_d = dram("stack_rows", [GROUPS // 2, AUX, SK], F32)
    out_t = dram("attended", [GROUPS, P, SQ], F32)
    x2_d = dram("x2", [B, SQ, D], F32)
    nh_d, nl_d = (dram(n, [B, P, NG, SQ], F32R) for n in ("x2_high", "x2_low"))
    scratch = (kh_d, kl_d, v_d, qh_d, ql_d, aux_d)
    with ExitStack() as whole:
        ident = whole.enter_context(nc.sbuf_tensor("ident", [P, P], F32))
        with ExitStack() as ctx:
            names = ("wq", "wk", "wv", "wki", "wvi")
            parts = {n: tuple(ctx.enter_context(nc.sbuf_tensor(f"{n}_{s}", [P, NG, D], F32R)) for s in ("high", "low")) for n in names}
            prepare_weights(nc, ident, [w_q, w_k, w_v, w_k_img, w_v_img], [parts[n] for n in names], "pw")
            rows = {"b_img": b_k_img, "b_txt": b_k, "b_q": b_q, "g_img": g_k_img, "g_txt": g_k, "g_q": g_q}
            project(nc, ident, x, ctx_in, lens, parts, rows, scratch)
        attend(nc, scratch, out_t, b_v, b_v_img)
        with ExitStack() as ctx:
            wo = tuple(ctx.enter_context(nc.sbuf_tensor(f"wo_{s}", [P, NG, D], F32R)) for s in ("high", "low"))
            prepare_weights(nc, ident, [w_o], [wo], "po")
            residual(nc, ident, x, out_t, wo, b_o, g_xattn, x2_d, nh_d, nl_d)
        with ExitStack() as ctx:
            t1 = ctx.enter_context(nc.sbuf_tensor("t1", [P, NG, FF], F32R))
            t2 = ctx.enter_context(nc.sbuf_tensor("t2", [P, NF, D], F32R))
            alpha = ctx.enter_context(nc.sbuf_tensor("alpha", [P, 2], F32))
            ternarize(nc, w1, w2, t1, t2, alpha)
            y_all = ctx.enter_context(nc.sbuf_tensor("y_all", [P, B * QT, D], F32))
            y_top = ctx.enter_context(nc.sbuf_tensor("y_top", [P, B * QT], F32))
            feed_forward(nc, nh_d, nl_d, t1, t2, alpha, b1, b2, y_all, y_top)
            quantize(nc, x2_d, y_all, y_top, g_ffn, out)


_INS = ["x", "ctx_2048", "_lenS2", "g_xattn", "g_ffn", "L0_xattn_w_q", "L0_xattn_b_q", "L0_xattn_w_k", "L0_xattn_b_k",
        "L0_xattn_w_v", "L0_xattn_b_v", "L0_xattn_w_k_img", "L0_xattn_b_k_img", "L0_xattn_w_v_img", "L0_xattn_b_v_img",
        "L0_xattn_w_o", "L0_xattn_b_o", "L0_xattn_g_q", "L0_xattn_g_k", "L0_xattn_g_k_img",
        "L0_ffn_W1", "L0_ffn_b1", "L0_ffn_W2", "L0_ffn_b2"]


def kernel(**inputs):
    import numpy as _np
    import concourse.bacc as _bacc
    from concourse import mybir as _mybir
    from concourse.bass_utils import run_bass_kernel_spmd as _run

    nc = _bacc.Bacc("TRN2", target_bir_lowering=False, num_devices=1)
    arrays, args = {}, []
    for name in _INS:
        v = _np.ascontiguousarray(inputs[name])
        arrays[f"in_{name}_dram"] = v
        args.append(nc.dram_tensor(f"in_{name}_dram", v.shape, _mybir.dt.from_np(v.dtype), kind="ExternalInput").ap())
    args.append(nc.dram_tensor("out_0_dram", (B, SQ, D), _mybir.dt.float32, kind="ExternalOutput").ap())
    flamingo_block(nc, *args)
    r = _run(nc, [arrays], core_ids=[0])
    return r.results[0]["out_0_dram"]
```
